# Optimizing a Trainium2 kernel written in Bass

```python
import numpy as np
import jax
import jax.numpy as jnp

def _softmax(x, axis=-1):
    return jax.nn.softmax(x, axis=axis)

def _gelu(x):
    return jax.nn.gelu(x, approximate=True)

def _silu(x):
    return jax.nn.silu(x)

def _sigmoid(x):
    return jax.nn.sigmoid(x)

def _layernorm(x, axis=-1, eps=1e-05):
    m = jnp.mean(x, axis=axis, keepdims=True)
    v = jnp.var(x, axis=axis, keepdims=True)
    return (x - m) / jnp.sqrt(v + eps)

def _scatter_add(tgt, idx, src, axis=0):
    return tgt.at[idx].add(src)

def _segment_sum(src, seg, n):
    return jax.ops.segment_sum(src, seg, n)
kernel_name = 'mk_dlrm_tower_d1_rec_r8_815cc1'

def setup_inputs(seed: int=0):
    np.random.seed(seed)
    _w = jnp.asarray

    def _rec_inputs():
        import jax
        import jax.numpy as jnp
        _tk = jax.random.key(seed)
        ids = jnp.stack([jax.random.randint(jax.random.fold_in(_tk, 200 + f), (2048,), 0, v, jnp.int32) for f, v in enumerate([125000, 12500, 12500, 1250, 1250, 12500, 1250, 12500, 1000, 12500, 1250, 1250, 12500, 1250, 1000, 1250, 12500, 1000, 12500, 1250, 1250, 1000, 1000, 1250, 1000, 1250])], axis=1)
        tbl_0 = 0.05 * jax.random.normal(jax.random.fold_in(_tk, 500 + 0), (125000, 128), jnp.float32)
        tbl_1 = 0.05 * jax.random.normal(jax.random.fold_in(_tk, 500 + 1), (12500, 128), jnp.float32)
        tbl_2 = 0.05 * jax.random.normal(jax.random.fold_in(_tk, 500 + 2), (12500, 128), jnp.float32)
        tbl_3 = 0.05 * jax.random.normal(jax.random.fold_in(_tk, 500 + 3), (1250, 128), jnp.float32)
        tbl_4 = 0.05 * jax.random.normal(jax.random.fold_in(_tk, 500 + 4), (1250, 128), jnp.float32)
        tbl_5 = 0.05 * jax.random.normal(jax.random.fold_in(_tk, 500 + 5), (12500, 128), jnp.float32)
        tbl_6 = 0.05 * jax.random.normal(jax.random.fold_in(_tk, 500 + 6), (1250, 128), jnp.float32)
        tbl_7 = 0.05 * jax.random.normal(jax.random.fold_in(_tk, 500 + 7), (12500, 128), jnp.float32)
        tbl_8 = 0.05 * jax.random.normal(jax.random.fold_in(_tk, 500 + 8), (1000, 128), jnp.float32)
        tbl_9 = 0.05 * jax.random.normal(jax.random.fold_in(_tk, 500 + 9), (12500, 128), jnp.float32)
        tbl_10 = 0.05 * jax.random.normal(jax.random.fold_in(_tk, 500 + 10), (1250, 128), jnp.float32)
        tbl_11 = 0.05 * jax.random.normal(jax.random.fold_in(_tk, 500 + 11), (1250, 128), jnp.float32)
        tbl_12 = 0.05 * jax.random.normal(jax.random.fold_in(_tk, 500 + 12), (12500, 128), jnp.float32)
        tbl_13 = 0.05 * jax.random.normal(jax.random.fold_in(_tk, 500 + 13), (1250, 128), jnp.float32)
        tbl_14 = 0.05 * jax.random.normal(jax.random.fold_in(_tk, 500 + 14), (1000, 128), jnp.float32)
        tbl_15 = 0.05 * jax.random.normal(jax.random.fold_in(_tk, 500 + 15), (1250, 128), jnp.float32)
        tbl_16 = 0.05 * jax.random.normal(jax.random.fold_in(_tk, 500 + 16), (12500, 128), jnp.float32)
        tbl_17 = 0.05 * jax.random.normal(jax.random.fold_in(_tk, 500 + 17), (1000, 128), jnp.float32)
        tbl_18 = 0.05 * jax.random.normal(jax.random.fold_in(_tk, 500 + 18), (12500, 128), jnp.float32)
        tbl_19 = 0.05 * jax.random.normal(jax.random.fold_in(_tk, 500 + 19), (1250, 128), jnp.float32)
        tbl_20 = 0.05 * jax.random.normal(jax.random.fold_in(_tk, 500 + 20), (1250, 128), jnp.float32)
        tbl_21 = 0.05 * jax.random.normal(jax.random.fold_in(_tk, 500 + 21), (1000, 128), jnp.float32)
        tbl_22 = 0.05 * jax.random.normal(jax.random.fold_in(_tk, 500 + 22), (1000, 128), jnp.float32)
        tbl_23 = 0.05 * jax.random.normal(jax.random.fold_in(_tk, 500 + 23), (1250, 128), jnp.float32)
        tbl_24 = 0.05 * jax.random.normal(jax.random.fold_in(_tk, 500 + 24), (1000, 128), jnp.float32)
        tbl_25 = 0.05 * jax.random.normal(jax.random.fold_in(_tk, 500 + 25), (1250, 128), jnp.float32)
        _rk = jax.random.fold_in(_tk, 7)
        r_dense_features = -0.000520686 + 1.00062 * jax.random.normal(jax.random.fold_in(_rk, 101), (2048, 128), jnp.float32)
        W_top1 = 0.0405887 * jax.random.normal(jax.random.fold_in(_tk, 801), (607, 512), jnp.float32)
        W_top2 = 0.0441942 * jax.random.normal(jax.random.fold_in(_tk, 802), (512, 256), jnp.float32)
        W_top3 = 0.0625 * jax.random.normal(jax.random.fold_in(_tk, 803), (256, 1), jnp.float32)
        b_top1 = jnp.zeros((512,), jnp.float32)
        b_top2 = jnp.zeros((256,), jnp.float32)
        return (r_dense_features, ids, tbl_0, tbl_1, tbl_2, tbl_3, tbl_4, tbl_5, tbl_6, tbl_7, tbl_8, tbl_9, tbl_10, tbl_11, tbl_12, tbl_13, tbl_14, tbl_15, tbl_16, tbl_17, tbl_18, tbl_19, tbl_20, tbl_21, tbl_22, tbl_23, tbl_24, tbl_25, W_top1, b_top1, W_top2, b_top2, W_top3)
    r_dense_features, ids, tbl_0, tbl_1, tbl_2, tbl_3, tbl_4, tbl_5, tbl_6, tbl_7, tbl_8, tbl_9, tbl_10, tbl_11, tbl_12, tbl_13, tbl_14, tbl_15, tbl_16, tbl_17, tbl_18, tbl_19, tbl_20, tbl_21, tbl_22, tbl_23, tbl_24, tbl_25, W_top1, b_top1, W_top2, b_top2, W_top3 = _rec_inputs()

    def _L0_rec_setup():
        import jax, jax.numpy as jnp
        import numpy as np
        B, F, D = (2048, 26, 128)
        key = jax.random.key(seed)
        k1, k2 = jax.random.split(key)
        dense_features = jax.random.normal(k1, (B, D), dtype=jnp.float32)
        sparse_values = jax.random.normal(k2, (B, F, D), dtype=jnp.float32)
        return {'dense_features': dense_features, 'sparse_values': sparse_values}
    _L0_rec_all = _L0_rec_setup()
    _L0_rec_in = {k: v for k, v in _L0_rec_all.items() if k in ()}
    del _L0_rec_all
    return {'r_dense_features': r_dense_features, 'ids': ids, 'tbl_0': tbl_0, 'tbl_1': tbl_1, 'tbl_2': tbl_2, 'tbl_3': tbl_3, 'tbl_4': tbl_4, 'tbl_5': tbl_5, 'tbl_6': tbl_6, 'tbl_7': tbl_7, 'tbl_8': tbl_8, 'tbl_9': tbl_9, 'tbl_10': tbl_10, 'tbl_11': tbl_11, 'tbl_12': tbl_12, 'tbl_13': tbl_13, 'tbl_14': tbl_14, 'tbl_15': tbl_15, 'tbl_16': tbl_16, 'tbl_17': tbl_17, 'tbl_18': tbl_18, 'tbl_19': tbl_19, 'tbl_20': tbl_20, 'tbl_21': tbl_21, 'tbl_22': tbl_22, 'tbl_23': tbl_23, 'tbl_24': tbl_24, 'tbl_25': tbl_25, 'W_top1': W_top1, 'b_top1': b_top1, 'W_top2': W_top2, 'b_top2': b_top2, 'W_top3': W_top3}

def reference(r_dense_features, ids, tbl_0, tbl_1, tbl_2, tbl_3, tbl_4, tbl_5, tbl_6, tbl_7, tbl_8, tbl_9, tbl_10, tbl_11, tbl_12, tbl_13, tbl_14, tbl_15, tbl_16, tbl_17, tbl_18, tbl_19, tbl_20, tbl_21, tbl_22, tbl_23, tbl_24, tbl_25, W_top1, b_top1, W_top2, b_top2, W_top3):
    import jax
    import jax.numpy as jnp

    def _L0_rec_ref(dense_features, sparse_values):
        import jax, jax.numpy as jnp
        import numpy as np
        B, F, D = (2048, 26, 128)
        sd = jnp.einsum('bfd,bd->bf', sparse_values, dense_features)
        ss = jnp.einsum('bfd,bgd->bfg', sparse_values, sparse_values)
        iu, ju = jnp.triu_indices(F, k=1)
        pairs = ss[:, iu, ju]
        return jnp.concatenate([dense_features, sd, pairs], axis=1)
    e = jnp.stack([tbl_0[ids[:, 0]], tbl_1[ids[:, 1]], tbl_2[ids[:, 2]], tbl_3[ids[:, 3]], tbl_4[ids[:, 4]], tbl_5[ids[:, 5]], tbl_6[ids[:, 6]], tbl_7[ids[:, 7]], tbl_8[ids[:, 8]], tbl_9[ids[:, 9]], tbl_10[ids[:, 10]], tbl_11[ids[:, 11]], tbl_12[ids[:, 12]], tbl_13[ids[:, 13]], tbl_14[ids[:, 14]], tbl_15[ids[:, 15]], tbl_16[ids[:, 16]], tbl_17[ids[:, 17]], tbl_18[ids[:, 18]], tbl_19[ids[:, 19]], tbl_20[ids[:, 20]], tbl_21[ids[:, 21]], tbl_22[ids[:, 22]], tbl_23[ids[:, 23]], tbl_24[ids[:, 24]], tbl_25[ids[:, 25]]], axis=1)
    z = _L0_rec_ref(r_dense_features, e)
    z = z.reshape(z.shape[0], -1)
    h = jnp.concatenate([z, r_dense_features], axis=1)
    h = jnp.maximum(h @ W_top1 + b_top1, 0.0)
    h = jnp.maximum(h @ W_top2 + b_top2, 0.0)
    y = h @ W_top3
    return y

_drawn_inputs = setup_inputs


def setup_inputs(seed=0):
    import zlib

    import numpy as np

    out = dict(_drawn_inputs(seed))
    spreads = {'b_top1': (0.0, 0.1), 'b_top2': (0.0, 0.1)}
    factors = {}
    for name, (base, spread) in spreads.items():
        noise = np.random.default_rng([zlib.crc32(name.encode()), seed]).standard_normal(out[name].shape)
        drawn = base * np.exp(spread * noise) if base else spread * noise
        out[name] = jnp.asarray(drawn.astype(out[name].dtype))
    for name, factor in factors.items():
        out[name] = (out[name] * factor).astype(out[name].dtype)
    return out
```

```python
from contextlib import ExitStack

import numpy as np

import concourse.bass as bass
import concourse.mybir as mybir

P = 128


def build(nc, io):
    fp32, i32 = mybir.dt.float32, mybir.dt.int32
    ALU = mybir.AluOpType
    ACT = mybir.ActivationFunctionType

    B, D = io["r_dense_features"].shape
    FIELDS = io["ids"].shape[1]
    N1, N2 = io["W_top2"].shape
    TILES = B // P
    NF = 1 + FIELDS
    PAD = 32
    PER = P // PAD
    PAIRS = NF * (NF - 1) // 2
    C1, C2 = N1 // P, N2 // P
    ZC = -(-PAIRS // P)
    zrows = [min(P, PAIRS - c * P) for c in range(ZC)]
    assert TILES % 2 == 0 and D == P

    groups = [list(range(f, min(f + 4, NF))) for f in range(0, NF, 4)]
    EVEN, ODD = len(groups[0::2]), len(groups[1::2])
    pieces, at = [], 0
    for f in range(NF - 1):
        g = f + 1
        while g < NF:
            n = min(NF - g, P - at % P)
            pieces.append((f, g, n, at // P, at % P))
            at, g = at + n, g + n
    HALF = 8
    HALVES = P // PER // HALF

    ctx = ExitStack()
    with ctx:
        def sb(name, shape, dt=fp32):
            return ctx.enter_context(nc.sbuf_tensor(name, shape, dt))

        def sem(name):
            return ctx.enter_context(nc.semaphore(name))

        ids = sb("ids_all", [P, TILES * FIELDS], i32)
        idx = [sb(f"idx{u}", [P, FIELDS], i32) for u in range(2)]
        rows = [sb(f"rows{u}", [P, NF * D]) for u in range(2)]
        dense = sb("dense", [P, TILES * D])
        ident = sb("ident", [P, P])
        feats = [sb(f"feats{u}", [P, P * PAD]) for u in range(2)]
        denseT = [sb(f"denseT{u}", [P, P]) for u in range(2)]
        dots = [sb(f"dots{u}", [PAD, (NF - 1) * P]) for u in range(2)]
        z = [sb(f"z{u}", [P, ZC * P]) for u in range(2)]
        w1a = sb("w1a", [P, N1])
        w1b = sb("w1b", [P, N1])
        w1d = sb("w1d", [P, N1])
        w1z = sb("w1z", [P, ZC * N1])
        w2 = sb("w2", [P, C1 * N2])
        w3 = sb("w3", [P, C2])
        b1 = sb("b1", [P, C1])
        b2 = sb("b2", [P, C2])
        h1 = sb("h1", [P, C1 * P])
        h2 = sb("h2", [P, C2 * P])
        y = sb("y", [P, TILES])

        tp = [ctx.enter_context(nc.psum_tensor(f"tp{b}", [P, 512], fp32)) for b in range(2)]
        gp = [ctx.enter_context(nc.psum_tensor(f"gp{b}", [P, HALF * P], fp32)) for b in range(2)]
        h1p = ctx.enter_context(nc.psum_tensor("h1p", [P, C1 * P], fp32))
        h2p = ctx.enter_context(nc.psum_tensor("h2p", [P, 512], fp32))
        yp = h2p[:, C2 * P:C2 * P + TILES]

        ids_loaded = sem("ids_loaded")
        dense_loaded = sem("dense_loaded")
        weights_loaded = sem("weights_loaded")
        ident_ready = sem("ident_ready")
        setup_done = sem("setup_done")
        idx_staged = sem("idx_staged")
        tiles_begun = sem("tiles_begun")
        gathered = [[sem(f"gathered{u}_{i}") for i in range(len(groups))] for u in range(2)]
        dense_staged = sem("dense_staged")
        tp_ready = [sem(f"tp_ready{b}") for b in range(2)]
        tp_copied = [sem(f"tp_copied{b}") for b in range(2)]
        gram_ready = sem("gram_ready")
        gram_copied_dve = sem("gram_copied_dve")
        gram_copied_act = sem("gram_copied_act")
        packed = [sem(f"packed{u}") for u in range(2)]
        h1_ready = sem("h1_ready")
        h1_relu = sem("h1_relu")
        h2_ready = sem("h2_ready")
        h2_relu = sem("h2_relu")
        y_ready = sem("y_ready")
        y_copied = sem("y_copied")
        stored = sem("stored")

        w1 = io["W_top1"]
        w1z_chunks = [(w1z[0:n, c * N1:(c + 1) * N1], w1[D + c * P:D + c * P + n, :]) for c, n in enumerate(zrows)]
        weight_loads = [
            (w1a[:, :], w1[0:D, :]),
            (w1b[:, :], w1[D + PAIRS:, :]),
            *w1z_chunks,
            (w2[:, :].rearrange("p (c n) -> p c n", c=C1), io["W_top2"].rearrange("(c p) n -> p c n", p=P)),
            (w3[:, :], io["W_top3"].rearrange("(c p) o -> p (c o)", p=P)),
            (b1[:, :], io["b_top1"].rearrange("(c p) -> p c", p=P)),
            (b2[:, :], io["b_top2"].rearrange("(c p) -> p c", p=P)),
        ]
        N_WEIGHTS = len(weight_loads)

        block = ctx.enter_context(nc.Block())

        def over_tiles(eng, tile):
            tile(0, 0, 0)
            with eng.Fori(0, TILES // 2 - 1) as r:
                tile(1, r, 2 * r + 1)
                tile(0, r + 1, 2 * r + 2)
            tile(1, TILES // 2 - 1, TILES - 1)

        @block.sync
        def _(sp):
            sp.dma_start(ids[:, :], io["ids"].rearrange("(p t) f -> p (t f)", p=P)).then_inc(ids_loaded, 16)
            sp.dma_start(dense[:, :], io["r_dense_features"].rearrange("(p t) d -> p (t d)", p=P)) \
              .then_inc(dense_loaded, 16)

            def pack(u, k, t):
                sp.wait_ge(gram_copied_dve, HALVES * (t + 1) + 2)
                sp.wait_ge(gram_copied_act, HALVES * (t + 1) + 2)
                for f, g, n, c, r0 in pieces:
                    sp.dma_start(z[u][r0:r0 + n, c * P:(c + 1) * P], dots[u][g:g + n, f * P:(f + 1) * P]) \
                      .then_inc(packed[u], 16)

            over_tiles(sp, pack)
            sp.wait_ge(y_copied, 1)
            sp.dma_start(io["out"].rearrange("(p t) o -> p (t o)", p=P), y[:, :]).then_inc(stored, 16)
            sp.wait_ge(stored, 16)

        @block.gpsimd
        def _(pool):
            def gather(u, k, t):
                pool.wait_ge(idx_staged, t + 1).then_inc(tiles_begun, 1)
                if not (isinstance(t, int) and t == 0):
                    pool.wait_ge(tp_copied[0], EVEN * (t - 1) + 1).then_inc(tiles_begun, 1)
                for i, group in enumerate(groups):
                    for f in group:
                        if f:
                            n = f - 1
                            pool.indirect_dma_start(
                                rows[u][:, f * D:(f + 1) * D], None, io[f"tbl_{n}"][:, :],
                                bass.IndirectOffsetOnAxis(idx[u][:, n:n + 1], 0)).then_inc(gathered[u][i], 16)

            pool.memset(ident[:, :], 0.0).then_inc(ident_ready, 1)
            pool.wait_ge(ident_ready, 1)
            pool.affine_select(out=ident[:, :], in_=ident[:, :], compare_op=ALU.not_equal, fill=1.0, base=0,
                               pattern=[[-1, P]], channel_multiplier=1).then_inc(ident_ready, 1)
            over_tiles(pool, gather)

        def copy_gram(eng, copy, u, h, js):
            dst = dots[u][:, :].rearrange("g (f c j) -> g c f j", f=NF - 1, j=PER)
            src = gp[h % 2][:, :].rearrange("p (c n) -> p c n", c=HALF)
            for j in js:
                last = copy(dst[0:NF, h * HALF:(h + 1) * HALF, :, j],
                            src[j * PAD:j * PAD + NF, :, j * (NF - 1):(j + 1) * (NF - 1)])
            return last

        def feature_copy(copy, u, i):
            group = groups[i]
            dst = feats[u][:, :].rearrange("d (b f) -> d f b", f=PAD)[:, group[0]:group[-1] + 1, :]
            return copy(dst, tp[i % 2][:, 0:len(group) * P].rearrange("d (f b) -> d f b", b=P))

        @block.vector
        def _(dve):
            def stage(u, t):
                dve.tensor_copy(idx[u][:, :], ids[:, bass.ds(t * FIELDS, FIELDS)]).then_inc(idx_staged, 1)
                dve.tensor_copy(rows[u][:, 0:D], dense[:, bass.ds(t * D, D)]).then_inc(dense_staged, 1)

            dve.wait_ge(ids_loaded, 16)
            dve.wait_ge(dense_loaded, 16)
            stage(0, 0)
            stage(1, 1)
            for u in range(2):
                dve.memset(feats[u][:, :], 0.0).then_inc(setup_done, 1)
            dve.sem_inc(tp_copied[0], 1)
            dve.sem_inc(gram_copied_dve, 2)
            dve.wait_ge(weights_loaded, 16 * N_WEIGHTS)
            dve.tensor_tensor(w1d[:, :], w1a[:, :], w1b[:, :], ALU.add).then_inc(setup_done, 1)
            dve.wait_ge(setup_done, 3)

            def transposed(u, k, t):
                for n, i in enumerate(range(0, len(groups), 2)):
                    dve.wait_ge(tp_ready[0], EVEN * t + n + 1)
                    if i == 0:
                        dve.tensor_copy(denseT[u][:, :], tp[0][:, 0:P])
                    feature_copy(dve.tensor_copy, u, i).then_inc(tp_copied[0], 1)

            def gram(u, k, t):
                for h in range(HALVES):
                    dve.wait_ge(gram_ready, HALVES * t + h + 1)
                    copy_gram(dve, dve.tensor_copy, u, h, (0, 1)).then_inc(gram_copied_dve, 1)

            def relu2(t):
                dve.wait_ge(h2_ready, t + 1)
                for c in range(C2):
                    dve.tensor_scalar(h2[:, c * P:(c + 1) * P], h2p[:, c * P:(c + 1) * P], b2[:, c:c + 1], 0.0,
                                      ALU.add, ALU.max).then_inc(h2_relu, 1)

            transposed(0, 0, 0)
            gram(0, 0, 0)

            def pair_tile(u, k, t):
                transposed(u, k, t)
                gram(u, k, t)
                relu2(t - 1)

            with dve.Fori(0, TILES // 2 - 1) as r:
                stage(0, 2 * r + 2)
                pair_tile(1, r, 2 * r + 1)
                stage(1, 2 * r + 3)
                pair_tile(0, r + 1, 2 * r + 2)
            pair_tile(1, TILES // 2 - 1, TILES - 1)
            relu2(TILES - 1)
            dve.wait_ge(y_ready, TILES)
            dve.tensor_copy(y[:, :], yp).then_inc(y_copied, 1)

        @block.scalar
        def _(act):
            with nc.allow_non_contiguous_dma(reason="biases and W_top3: a few words per partition, once"):
                for dst, src in weight_loads:
                    act.dma_start(dst, src).then_inc(weights_loaded, 16)
            act.sem_inc(tp_copied[1], 1)
            act.sem_inc(gram_copied_act, 2)
            act.wait_ge(weights_loaded, 16 * N_WEIGHTS)
            act.wait_ge(setup_done, 3)

            def copy(dst, src):
                return act.activation(dst, src, ACT.Copy)

            def relu1(t):
                act.wait_ge(h1_ready, t + 1)
                for c in range(C1):
                    act.activation(h1[:, c * P:(c + 1) * P], h1p[:, c * P:(c + 1) * P], ACT.Relu,
                                   bias=b1[:, c:c + 1]).then_inc(h1_relu, 1)

            def tile(u, k, t):
                for n, i in enumerate(range(1, len(groups), 2)):
                    act.wait_ge(tp_ready[1], ODD * t + n + 1)
                    feature_copy(copy, u, i).then_inc(tp_copied[1], 1)
                for h in range(HALVES):
                    act.wait_ge(gram_ready, HALVES * t + h + 1)
                    copy_gram(act, copy, u, h, (2, 3)).then_inc(gram_copied_act, 1)
                if not (isinstance(t, int) and t == 0):
                    relu1(t - 1)

            over_tiles(act, tile)
            relu1(TILES - 1)

        @block.tensor
        def _(pe):
            pe.wait_ge(ident_ready, 2)
            pe.wait_ge(setup_done, 3)
            pe.wait_ge(weights_loaded, 16 * N_WEIGHTS)

            def transposes(u, k, t):
                for i, group in enumerate(groups):
                    b, per, n = (0, EVEN, i // 2) if i % 2 == 0 else (1, ODD, i // 2)
                    pe.wait_ge(gathered[u][i], 16 * sum(f > 0 for f in group) * (k + 1))
                    pe.wait_ge(tp_copied[b], per * t + n + 1)
                    if i == 0:
                        pe.wait_ge(dense_staged, t + 1)
                    for m, f in enumerate(group):
                        last = pe.transpose(tp[b][:, m * P:(m + 1) * P], rows[u][:, f * D:(f + 1) * D], ident[:, :])
                    last.then_inc(tp_ready[b], 1)

            def gram(u, k, t):
                pe.wait_ge(tp_copied[0], EVEN * (t + 1) + 1)
                pe.wait_ge(tp_copied[1], ODD * (t + 1) + 1)
                batch = feats[u][:, :].rearrange("d (b f) -> d b f", f=PAD)
                for h in range(HALVES):
                    pe.wait_ge(gram_copied_dve, HALVES * t + h + 1)
                    pe.wait_ge(gram_copied_act, HALVES * t + h + 1)
                    for c in range(HALF):
                        b = (h * HALF + c) * PER
                        last = pe.matmul(gp[h % 2][:, c * P:c * P + PER * (NF - 1)],
                                         feats[u][:, b * PAD:(b + PER) * PAD], batch[:, b:b + PER, 0:NF - 1],
                                         start=True, stop=True)
                    last.then_inc(gram_ready, 1)

            def layers(u, k, t):
                pe.wait_ge(packed[u], 16 * len(pieces) * (k + 1))
                for c in range(C1):
                    n = slice(c * P, (c + 1) * P)
                    pe.matmul(h1p[:, n], w1d[:, n], denseT[u][:, :], start=True, stop=False)
                    for q in range(ZC):
                        last = pe.matmul(h1p[:, n], w1z[0:zrows[q], q * N1 + c * P:q * N1 + (c + 1) * P],
                                         z[u][0:zrows[q], q * P:(q + 1) * P], start=False, stop=q == ZC - 1)
                last.then_inc(h1_ready, 1)
                pe.wait_ge(h1_relu, C1 * (t + 1))
                for c in range(C2):
                    for q in range(C1):
                        last = pe.matmul(h2p[:, c * P:(c + 1) * P], w2[:, q * N2 + c * P:q * N2 + (c + 1) * P],
                                         h1[:, q * P:(q + 1) * P], start=q == 0, stop=q == C1 - 1)
                last.then_inc(h2_ready, 1)
                pe.wait_ge(h2_relu, C2 * (t + 1))
                for c in range(C2):
                    last = pe.matmul(yp[:, bass.ds(t, 1)], h2[:, c * P:(c + 1) * P], w3[:, c:c + 1],
                                     start=c == 0, stop=c == C2 - 1)
                last.then_inc(y_ready, 1)

            def tile(u, k, t):
                transposes(u, k, t)
                gram(u, k, t)
                if not (isinstance(t, int) and t == 0):
                    layers(1 - u, k if u else k - 1, t - 1)

            over_tiles(pe, tile)
            layers(1, TILES // 2 - 1, TILES - 1)


def kernel(**inputs):
    import concourse.bacc as bacc
    from concourse.bass_utils import run_bass_kernel_spmd

    nc = bacc.Bacc("TRN2", target_bir_lowering=False, num_devices=1)
    arrays, io = {}, {}
    for name, a in inputs.items():
        a = np.ascontiguousarray(a)
        arrays["in_" + name] = a
        io[name] = nc.dram_tensor("in_" + name, a.shape, mybir.dt.from_np(a.dtype), kind="ExternalInput").ap()
    batch = inputs["ids"].shape[0]
    io["out"] = nc.dram_tensor("out_0", (batch, 1), mybir.dt.float32, kind="ExternalOutput").ap()
    build(nc, io)
    r = run_bass_kernel_spmd(nc, [arrays], core_ids=[0])
    return r.results[0]["out_0"]
```

```python
from contextlib import ExitStack

import numpy as np

import concourse.bass as bass
import concourse.mybir as mybir

P = 128


def build(nc, io):
    fp32, i32, bf16, fp16 = mybir.dt.float32, mybir.dt.int32, mybir.dt.bfloat16, mybir.dt.float16
    ALU = mybir.AluOpType
    ACT = mybir.ActivationFunctionType

    B, D = io["r_dense_features"].shape
    FIELDS = io["ids"].shape[1]
    N1, N2 = io["W_top2"].shape
    TILES = B // P
    NF = 1 + FIELDS
    PAD = 32
    PER = P // PAD
    PAIRS = NF * (NF - 1) // 2
    C1, C2 = N1 // P, N2 // P
    ZC = -(-PAIRS // P)
    zrows = [min(P, PAIRS - c * P) for c in range(ZC)]
    assert TILES % 2 == 0 and TILES >= 6 and D == P

    V, K = 1000, 125
    CH = V // K
    hot = [1 + i for i in range(FIELDS) if io[f"tbl_{i}"].shape[0] == V][-4:]
    HOT = len(hot)
    H0, H1 = hot[0] - 1, hot[-1]
    cold = [f for f in range(NF) if f not in hot]
    groups = [cold[i:i + 4] for i in range(0, len(cold), 4)]
    assert len(groups) == 6 and HOT == 4 and V <= 2048

    TURNS = (("onehot", 1, 3, 4), (0, 2, "ids", 5))
    BEFORE = (1, 2)
    AHEAD = {"onehot": 1, "ids": 2}

    def turn(b, t, what):
        at = TURNS[b].index(what)
        n = BEFORE[b] + len(TURNS[b]) * t + at
        if isinstance(t, int):
            for s in range(max(0, t - 2), t + 1):
                for w in TURNS[b] if s < t else TURNS[b][:at]:
                    n -= w in AHEAD and s + AHEAD[w] >= TILES
        return n

    pieces, at = [], 0
    for f in range(NF - 1):
        g = f + 1
        while g < NF:
            n = min(NF - g, P - at % P)
            pieces.append((f, g, n, at // P, at % P))
            at, g = at + n, g + n
    BY_POOL = 10
    HALF = 8
    HALVES = P // PER // HALF

    def progressions(fs):
        i = 0
        while i < len(fs):
            step = fs[i + 1] - fs[i] if i + 1 < len(fs) else 1
            n = 1
            while i + n < len(fs) and fs[i + n] - fs[i + n - 1] == step:
                n += 1
            yield i, fs[i], n, step
            i += n

    ctx = ExitStack()
    with ctx:
        def sb(name, shape, dt=fp32):
            return ctx.enter_context(nc.sbuf_tensor(name, shape, dt))

        def sem(name):
            return ctx.enter_context(nc.semaphore(name))

        ids = sb("ids_all", [P, TILES * FIELDS], i32)
        idx = [sb(f"idx{u}", [P, FIELDS], i32) for u in range(2)]
        ids16 = [sb(f"ids16_{u}", [P, H1 - H0], fp16) for u in range(2)]
        rows = [sb(f"rows{u}", [P, NF * D]) for u in range(2)]
        dense = sb("dense", [P, TILES * D])
        ident = sb("ident", [P, P])
        ident16 = sb("ident16", [P, P], fp16)
        table = sb("table", [K, HOT * CH * D])
        parts = [sb(f"table_part{i}", [K, HOT * CH * D], bf16) for i in range(3)]
        row_of = sb("row_of", [P, CH], i32)
        row_of_f = sb("row_of_f", [P, CH])
        idsb = sb("idsb", [P, HOT * P], fp16)
        onehot = sb("onehot", [K, CH * HOT * P], bf16)
        feats = [sb(f"feats{u}", [P, P * PAD]) for u in range(2)]
        denseT = [sb(f"denseT{u}", [P, P]) for u in range(2)]
        dots = [sb(f"dots{u}", [PAD, (NF - 1) * P]) for u in range(2)]
        z = [sb(f"z{u}", [P, ZC * P]) for u in range(2)]
        w1a = sb("w1a", [P, N1])
        w1b = sb("w1b", [P, N1])
        w1d = sb("w1d", [P, N1])
        w1z = sb("w1z", [P, ZC * N1])
        w2 = sb("w2", [P, C1 * N2])
        w3 = sb("w3", [P, C2])
        b1 = sb("b1", [P, C1])
        b2 = sb("b2", [P, C2])
        h1 = sb("h1", [P, C1 * P])
        h2 = sb("h2", [P, C2 * P])
        y = sb("y", [P, TILES])

        tp = [ctx.enter_context(nc.psum_tensor(f"tp{b}", [P, 512], fp32)) for b in range(2)]
        gp = [ctx.enter_context(nc.psum_tensor(f"gp{b}", [P, HALF * P], fp32)) for b in range(2)]
        h1p = ctx.enter_context(nc.psum_tensor("h1p", [P, C1 * P], fp32))
        h2p = ctx.enter_context(nc.psum_tensor("h2p", [P, 512], fp32))
        yp = h2p[:, C2 * P:C2 * P + TILES]

        ids_loaded = sem("ids_loaded")
        dense_loaded = sem("dense_loaded")
        table_loaded = [sem(f"table_loaded{s}") for s in range(HOT)]
        weights_loaded = sem("weights_loaded")
        row_of_ready = sem("row_of_ready")
        ident_ready = sem("ident_ready")
        setup_done = sem("setup_done")
        table_split = sem("table_split")
        w1d_ready = sem("w1d_ready")
        idx_staged = sem("idx_staged")
        dense_staged = sem("dense_staged")
        ids16_staged = sem("ids16_staged")
        tiles_begun = sem("tiles_begun")
        gathered = [[sem(f"gathered{u}_{i}") for i in range(len(groups))] for u in range(2)]
        tp_ready = [sem(f"tp_ready{b}") for b in range(2)]
        tp_copied = [sem(f"tp_copied{b}") for b in range(2)]
        onehot_ready = sem("onehot_ready")
        gram_ready = sem("gram_ready")
        gram_copied_dve = sem("gram_copied_dve")
        gram_copied_act = sem("gram_copied_act")
        packed = [sem(f"packed{u}") for u in range(2)]
        packed_by_pool = sem("packed_by_pool")
        h1_ready = sem("h1_ready")
        h1_relu = sem("h1_relu")
        h2_ready = sem("h2_ready")
        h2_relu = sem("h2_relu")
        y_ready = sem("y_ready")
        y_copied = sem("y_copied")
        stored = sem("stored")

        w1 = io["W_top1"]
        weight_loads = [
            (w1a[:, :], w1[0:D, :]),
            (w1b[:, :], w1[D + PAIRS:, :]),
            *[(w1z[0:n, c * N1:(c + 1) * N1], w1[D + c * P:D + c * P + n, :]) for c, n in enumerate(zrows)],
            (w2[:, :].rearrange("p (c n) -> p c n", c=C1), io["W_top2"].rearrange("(c p) n -> p c n", p=P)),
            (w3[:, :], io["W_top3"].rearrange("(c p) o -> p (c o)", p=P)),
            (b1[:, :], io["b_top1"].rearrange("(c p) -> p c", p=P)),
            (b2[:, :], io["b_top2"].rearrange("(c p) -> p c", p=P)),
        ]

        block = ctx.enter_context(nc.Block())

        def over_tiles(eng, tile, between=None):
            tile(0, 0, 0)
            tile(1, 0, 1)
            if between:
                between()
            with eng.Fori(1, TILES // 2 - 1) as k:
                tile(0, k, 2 * k)
                tile(1, k, 2 * k + 1)
            tile(0, TILES // 2 - 1, TILES - 2)
            tile(1, TILES // 2 - 1, TILES - 1)

        def there(t):
            return not isinstance(t, int) or 0 <= t < TILES

        def pack_piece(eng, u, piece, done):
            f, g, n, c, r0 = piece
            eng.dma_start(z[u][r0:r0 + n, c * P:(c + 1) * P], dots[u][g:g + n, f * P:(f + 1) * P]) \
               .then_inc(done, 16)

        @block.sync
        def _(sp):
            sp.dma_start(ids[:, :], io["ids"].rearrange("(p t) f -> p (t f)", p=P)).then_inc(ids_loaded, 16)
            for s, f in enumerate(hot):
                sp.dma_start(table[:, s * CH * D:(s + 1) * CH * D].rearrange("k (c d) -> k c d", c=CH),
                             io[f"tbl_{f - 1}"].rearrange("(c k) d -> k c d", k=K)).then_inc(table_loaded[s], 16)
                if s == 0:
                    sp.dma_start(dense[:, :], io["r_dense_features"].rearrange("(p t) d -> p (t d)", p=P)) \
                      .then_inc(dense_loaded, 16)

            def pack(u, k, t):
                sp.wait_ge(gram_copied_dve, HALVES * (t + 1) + 2)
                sp.wait_ge(gram_copied_act, HALVES * (t + 1) + 2)
                last = isinstance(t, int) and t == TILES - 1
                for piece in pieces[:-BY_POOL] if last else pieces:
                    pack_piece(sp, u, piece, packed[u])

            over_tiles(sp, pack)
            sp.wait_ge(y_copied, 1)
            sp.dma_start(io["out"].rearrange("(p t) o -> p (t o)", p=P), y[:, :]).then_inc(stored, 16)
            sp.wait_ge(stored, 16)

        @block.gpsimd
        def _(pool):
            def gather(u, k, t):
                pool.wait_ge(idx_staged, t + 1).then_inc(tiles_begun, 1)
                for i, group in enumerate(groups):
                    for f in group:
                        if f:
                            pool.indirect_dma_start(
                                rows[u][:, f * D:(f + 1) * D], None, io[f"tbl_{f - 1}"][:, :],
                                bass.IndirectOffsetOnAxis(idx[u][:, f - 1:f], 0)).then_inc(gathered[u][i], 16)

            pool.iota(row_of[:, :], [[K, CH]], base=0, channel_multiplier=1).then_inc(row_of_ready, 1)
            pool.memset(ident[:, :], 0.0).then_inc(ident_ready, 1)
            pool.wait_ge(ident_ready, 1)
            pool.affine_select(out=ident[:, :], in_=ident[:, :], compare_op=ALU.not_equal, fill=1.0, base=0,
                               pattern=[[-1, P]], channel_multiplier=1).then_inc(ident_ready, 1)
            over_tiles(pool, gather)
            pool.wait_ge(gram_copied_dve, HALVES * TILES + 2)
            pool.wait_ge(gram_copied_act, HALVES * TILES + 2)
            for piece in pieces[-BY_POOL:]:
                pack_piece(pool, 1, piece, packed_by_pool)

        def copy_gram(copy, u, h, js):
            dst = dots[u][:, :].rearrange("g (f c j) -> g c f j", f=NF - 1, j=PER)
            src = gp[h % 2][:, :].rearrange("p (c n) -> p c n", c=HALF)
            for j in js:
                last = copy(dst[0:NF, h * HALF:(h + 1) * HALF, :, j],
                            src[j * PAD:j * PAD + NF, :, j * (NF - 1):(j + 1) * (NF - 1)])
            return last

        def copy_features(copy, u, b, fs):
            src = tp[b][:, :].rearrange("d (f b) -> d f b", b=P)
            dst = feats[u][:, :].rearrange("d (b f) -> d f b", f=PAD)
            for at, f, n, step in progressions(fs):
                last = copy(dst[:, f:f + (n - 1) * step + 1:step, :], src[:, at:at + n, :])
            return last

        @block.vector
        def _(dve):
            copy = dve.tensor_copy

            def stage_rows(u, t):
                copy(idx[u][:, :], ids[:, bass.ds(t * FIELDS, FIELDS)]).then_inc(idx_staged, 1)

            def stage_dense(u, t):
                copy(rows[u][:, 0:D], dense[:, bass.ds(t * D, D)]).then_inc(dense_staged, 1)

            def stage_ids16(u, t):
                copy(ids16[u][:, :], ids[:, bass.ds(t * FIELDS + H0, H1 - H0)]).then_inc(ids16_staged, 1)

            def make_onehot(t):
                dve.wait_ge(tp_copied[1], turn(1, t - 2, "ids") + 2 if not isinstance(t, int) or t > 1 else t + 2)
                for c in range(CH):
                    last = dve.tensor_scalar(onehot[:, c * HOT * P:(c + 1) * HOT * P], idsb[0:K, :],
                                             row_of_f[0:K, c:c + 1], None, ALU.is_equal)
                last.then_inc(onehot_ready, 1)

            dve.sem_inc(tp_copied[0], 1)
            dve.sem_inc(gram_copied_dve, 2)
            dve.wait_ge(ids_loaded, 16)
            for u in range(2):
                stage_rows(u, u)
            for u in range(2):
                stage_ids16(u, u)
            for u in range(2):
                dve.memset(feats[u][:, :].rearrange("d (b f) -> d b f", f=PAD)[:, :, NF:], 0.0).then_inc(setup_done, 1)
            dve.wait_ge(ident_ready, 2)
            copy(ident16[:, :], ident[:, :]).then_inc(setup_done, 1)
            dve.wait_ge(row_of_ready, 1)
            copy(row_of_f[:, :], row_of[:, :]).then_inc(setup_done, 1)
            dve.wait_ge(setup_done, 4)
            dve.wait_ge(dense_loaded, 16)
            for u in range(2):
                stage_dense(u, u)
            make_onehot(0)
            hi, mid, lo = parts
            for s in range(HOT):
                cols = slice(s * CH * D, (s + 1) * CH * D)
                dve.wait_ge(table_loaded[s], 16)
                copy(hi[:, cols], table[:, cols]).then_inc(table_split, 1)
                dve.wait_ge(table_split, 4 * s + 1)
                dve.tensor_tensor(table[:, cols], table[:, cols], hi[:, cols], ALU.subtract).then_inc(table_split, 1)
                dve.wait_ge(table_split, 4 * s + 2)
                copy(mid[:, cols], table[:, cols]).then_inc(table_split, 1)
                dve.wait_ge(table_split, 4 * s + 3)
                dve.tensor_tensor(lo[:, cols], table[:, cols], mid[:, cols], ALU.subtract).then_inc(table_split, 1)

            def onehot_features(u, t):
                before = turn(0, t - 1, "onehot") if not isinstance(t, int) or t else 0
                dve.wait_ge(tp_ready[0], before + 1)
                copy_features(copy, u, 0, hot).then_inc(tp_copied[0], 1)

            onehot_features(0, 0)
            make_onehot(1)
            dve.wait_ge(weights_loaded, 16 * len(weight_loads))
            dve.tensor_tensor(w1d[:, :], w1a[:, :], w1b[:, :], ALU.add).then_inc(w1d_ready, 1)

            def relu2(t):
                dve.wait_ge(h2_ready, t + 1)
                for c in range(C2):
                    dve.tensor_scalar(h2[:, c * P:(c + 1) * P], h2p[:, c * P:(c + 1) * P], b2[:, c:c + 1], 0.0,
                                      ALU.add, ALU.max).then_inc(h2_relu, 1)

            def tile(u, k, t):
                if there(t + 2):
                    stage_ids16(u, t + 2)
                if there(t + 1):
                    onehot_features(1 - u, t + 1)
                if there(t - 2):
                    relu2(t - 2)
                for i in (1, 3, 4):
                    dve.wait_ge(tp_ready[0], turn(0, t, i) + 1)
                    copy_features(copy, u, 0, groups[i]).then_inc(tp_copied[0], 1)
                if there(t + 2):
                    make_onehot(t + 2)
                for h in range(HALVES):
                    dve.wait_ge(gram_ready, HALVES * t + h + 1)
                    copy_gram(copy, u, h, (0, 1)).then_inc(gram_copied_dve, 1)
                    if h == 0 and there(t + 2):
                        stage_rows(u, t + 2)
                        stage_dense(u, t + 2)

            over_tiles(dve, tile)
            relu2(TILES - 2)
            relu2(TILES - 1)
            dve.wait_ge(y_ready, TILES)
            copy(y[:, :], yp).then_inc(y_copied, 1)

        @block.scalar
        def _(act):
            with nc.allow_non_contiguous_dma(reason="biases and W_top3: a few words per partition, once"):
                for dst, src in weight_loads:
                    act.dma_start(dst, src).then_inc(weights_loaded, 16)
            act.sem_inc(tp_copied[1], 1)
            act.sem_inc(gram_copied_act, 2)
            act.wait_ge(setup_done, 4)

            def copy(dst, src):
                return act.activation(dst, src, ACT.Copy)

            def broadcast_ids(turns_before):
                act.wait_ge(tp_ready[1], turns_before + 1)
                copy(idsb[:, :], tp[1][:, :]).then_inc(tp_copied[1], 1)

            broadcast_ids(0)
            broadcast_ids(1)

            def relu1(t):
                act.wait_ge(h1_ready, t + 1)
                for c in range(C1):
                    act.activation(h1[:, c * P:(c + 1) * P], h1p[:, c * P:(c + 1) * P], ACT.Relu,
                                   bias=b1[:, c:c + 1]).then_inc(h1_relu, 1)

            def tile(u, k, t):
                if there(t - 2):
                    relu1(t - 2)
                for what in TURNS[1]:
                    if what == "ids":
                        if there(t + 2):
                            broadcast_ids(turn(1, t, "ids"))
                        continue
                    act.wait_ge(tp_ready[1], turn(1, t, what) + 1)
                    if what == 0:
                        copy(denseT[u][:, :], tp[1][:, 0:P])
                    copy_features(copy, u, 1, groups[what]).then_inc(tp_copied[1], 1)
                for h in range(HALVES):
                    act.wait_ge(gram_ready, HALVES * t + h + 1)
                    copy_gram(copy, u, h, (2, 3)).then_inc(gram_copied_act, 1)

            def weights_here():
                act.wait_ge(weights_loaded, 16 * len(weight_loads))

            over_tiles(act, tile, weights_here)
            relu1(TILES - 2)
            relu1(TILES - 1)

        @block.tensor
        def _(pe):
            def broadcast_ids(u, t, turns_before):
                pe.wait_ge(ids16_staged, t + 1)
                pe.wait_ge(tp_copied[1], turns_before + 1)
                for s, f in enumerate(hot):
                    n = f - 1 - H0
                    last = pe.matmul(tp[1][:, s * P:(s + 1) * P], ids16[u][:, n:n + 1].to_broadcast([P, P]),
                                     ident16[:, :], start=True, stop=True)
                last.then_inc(tp_ready[1], 1)

            def onehot_products(t, turns_before):
                pe.wait_ge(onehot_ready, t + 1)
                pe.wait_ge(tp_copied[0], turns_before + 1)
                for s in range(HOT):
                    for c in range(CH):
                        for i, part in enumerate(parts):
                            at = (s * CH + c) * D
                            hots = (c * HOT + s) * P
                            last = pe.matmul(tp[0][:, s * P:(s + 1) * P], part[:, at:at + D],
                                             onehot[:, hots:hots + P], start=c == 0 and i == 0,
                                             stop=c == CH - 1 and i == 2)
                last.then_inc(tp_ready[0], 1)

            def transposes(u, k, t, i):
                b = 0 if i in TURNS[0] else 1
                if i == 0:
                    pe.wait_ge(dense_staged, t + 1)
                pe.wait_ge(gathered[u][i], 16 * sum(f > 0 for f in groups[i]) * (k + 1))
                pe.wait_ge(tp_copied[b], turn(b, t, i) + 1)
                for m, f in enumerate(groups[i]):
                    last = pe.transpose(tp[b][:, m * P:(m + 1) * P], rows[u][:, f * D:(f + 1) * D], ident[:, :])
                last.then_inc(tp_ready[b], 1)

            def gram(u, t):
                pe.wait_ge(tp_copied[0], turn(0, t, 4) + 2)
                pe.wait_ge(tp_copied[1], turn(1, t, 5) + 2)
                batch = feats[u][:, :].rearrange("d (b f) -> d b f", f=PAD)
                for h in range(HALVES):
                    pe.wait_ge(gram_copied_dve, HALVES * t + h + 1)
                    pe.wait_ge(gram_copied_act, HALVES * t + h + 1)
                    for c in range(HALF):
                        b = (h * HALF + c) * PER
                        last = pe.matmul(gp[h % 2][:, c * P:c * P + PER * (NF - 1)],
                                         feats[u][:, b * PAD:(b + PER) * PAD], batch[:, b:b + PER, 0:NF - 1],
                                         start=True, stop=True)
                    last.then_inc(gram_ready, 1)

            def layer1(u, k):
                last = u == 1 and isinstance(k, int) and k == TILES // 2 - 1
                pe.wait_ge(packed[u], 16 * (len(pieces) * (k + 1) - (BY_POOL if last else 0)))
                if last:
                    pe.wait_ge(packed_by_pool, 16 * BY_POOL)
                for c in range(C1):
                    n = slice(c * P, (c + 1) * P)
                    pe.matmul(h1p[:, n], w1d[:, n], denseT[u][:, :], start=True, stop=False)
                    for q in range(ZC):
                        last = pe.matmul(h1p[:, n], w1z[0:zrows[q], q * N1 + c * P:q * N1 + (c + 1) * P],
                                         z[u][0:zrows[q], q * P:(q + 1) * P], start=False, stop=q == ZC - 1)
                last.then_inc(h1_ready, 1)

            def layer2(t):
                pe.wait_ge(h1_relu, C1 * (t + 1))
                for c in range(C2):
                    for q in range(C1):
                        last = pe.matmul(h2p[:, c * P:(c + 1) * P], w2[:, q * N2 + c * P:q * N2 + (c + 1) * P],
                                         h1[:, q * P:(q + 1) * P], start=q == 0, stop=q == C1 - 1)
                last.then_inc(h2_ready, 1)

            def layer3(t):
                pe.wait_ge(h2_relu, C2 * (t + 1))
                for c in range(C2):
                    last = pe.matmul(yp[:, bass.ds(t, 1)], h2[:, c * P:(c + 1) * P], w3[:, c:c + 1],
                                     start=c == 0, stop=c == C2 - 1)
                last.then_inc(y_ready, 1)

            pe.wait_ge(ident_ready, 2)
            pe.wait_ge(setup_done, 4)
            broadcast_ids(0, 0, 0)
            pe.wait_ge(table_split, 4 * HOT)
            onehot_products(0, 0)
            broadcast_ids(1, 1, 1)

            def tile(u, k, t):
                behind = there(t - 2)
                if behind:
                    layer1(u, k - 1)
                if there(t + 1):
                    onehot_products(t + 1, turn(0, t, "onehot"))
                if behind:
                    layer2(t - 2)
                for i in range(4):
                    transposes(u, k, t, i)
                if there(t + 2):
                    broadcast_ids(u, t + 2, turn(1, t, "ids"))
                for i in (4, 5):
                    transposes(u, k, t, i)
                if behind:
                    layer3(t - 2)
                gram(u, t)

            def weights_here():
                pe.wait_ge(w1d_ready, 1)
                pe.wait_ge(weights_loaded, 16 * len(weight_loads))

            over_tiles(pe, tile, weights_here)
            for u in range(2):
                layer1(u, TILES // 2 - 1)
                layer2(TILES - 2 + u)
                layer3(TILES - 2 + u)


def kernel(**inputs):
    import concourse.bacc as bacc
    from concourse.bass_utils import run_bass_kernel_spmd

    nc = bacc.Bacc("TRN2", target_bir_lowering=False, num_devices=1)
    arrays, io = {}, {}
    for name, a in inputs.items():
        a = np.ascontiguousarray(a)
        arrays["in_" + name] = a
        io[name] = nc.dram_tensor("in_" + name, a.shape, mybir.dt.from_np(a.dtype), kind="ExternalInput").ap()
    batch = inputs["ids"].shape[0]
    io["out"] = nc.dram_tensor("out_0", (batch, 1), mybir.dt.float32, kind="ExternalOutput").ap()
    build(nc, io)
    r = run_bass_kernel_spmd(nc, [arrays], core_ids=[0])
    return r.results[0]["out_0"]
```

```python
from contextlib import ExitStack

import numpy as np

import concourse.bass as bass
import concourse.mybir as mybir

P = 128


def hot_features(table_rows):
    return [1 + i for i, n in enumerate(table_rows) if n == 1000][-5:]


def build(nc, io):
    fp32, i32, bf16, fp16 = mybir.dt.float32, mybir.dt.int32, mybir.dt.bfloat16, mybir.dt.float16
    ALU = mybir.AluOpType
    ACT = mybir.ActivationFunctionType

    D, B = io["dense_by_tile"].shape
    FIELDS = io["ids"].shape[1]
    N1, N2 = io["W_top2"].shape
    TILES = B // P
    NF = 1 + FIELDS
    PAD = 32
    PER = P // PAD
    PAIRS = NF * (NF - 1) // 2
    C1, C2 = N1 // P, N2 // P
    assert TILES % 2 == 0 and TILES >= 6 and D == P

    V, K = 1000, 125
    CH = V // K
    hot = hot_features([io[f"tbl_{i}"].shape[0] for i in range(FIELDS)])
    HOT = len(hot)
    HA = 2
    hot_of = (hot[:HA], hot[HA:])
    cold = [f for f in range(1, NF) if f not in hot]
    groups = [cold[i:i + 4] for i in range(0, len(cold), 4)]
    assert len(groups) == 6 and HOT == 5 and V <= 2048

    TURNS = ((0, 2, 4, "onehot"), (1, 3, 5, "onehot"))

    def turn(b, t, what):
        at = TURNS[b].index(what)
        if isinstance(t, int) and t == 0 and what != "onehot":
            return at
        return 1 + len(TURNS[b]) * t + at

    def onehot_turn(b, t):
        return turn(b, t - 1, "onehot") if not isinstance(t, int) or t > 0 else len(TURNS[b]) - 1

    pieces, c, row = [], 0, 0
    zrows = []
    for f in range(0, NF - 1, 3):
        width = min(3, NF - 1 - f)
        g = f + 1
        while g < NF:
            n = min(NF - g, (P - row) // width)
            if n == 0:
                zrows.append(row)
                c, row = c + 1, 0
                continue
            pieces.append((f, width, g, n, c, row))
            g, row = g + n, row + n * width
    zrows.append(row)
    ZC = len(zrows)
    assert ZC == -(-PAIRS // P)
    LAYER1_AFTER = (0, 1, 3, 5)
    BY_POOL = 4
    HALF = 8
    HALVES = P // PER // HALF

    def progressions(fs):
        i = 0
        while i < len(fs):
            step = fs[i + 1] - fs[i] if i + 1 < len(fs) else 1
            n = 1
            while i + n < len(fs) and fs[i + n] - fs[i + n - 1] == step:
                n += 1
            yield i, fs[i], n, step
            i += n

    ctx = ExitStack()
    with ctx:
        def sb(name, shape, dt=fp32):
            return ctx.enter_context(nc.sbuf_tensor(name, shape, dt))

        def sem(name):
            return ctx.enter_context(nc.semaphore(name))

        ids = sb("ids_all", [P, TILES * FIELDS], i32)
        idx = [sb(f"idx{u}", [P, FIELDS], i32) for u in range(2)]
        rows = [sb(f"rows{u}", [P, NF * D]) for u in range(2)]
        dense = sb("dense", [P, TILES * P])
        ident = sb("ident", [P, P])
        table = sb("table", [K, HOT * CH * D])
        parts = [sb(f"table_part{i}", [K, HOT * CH * D], bf16) for i in range(3)]
        row_of = sb("row_of", [P, CH], i32)
        row_of16 = sb("row_of16", [K, CH * P], fp16)
        hot_ids = [sb(f"hot_ids{u}", [K, HOT * P], i32) for u in range(2)]
        hot_ids16 = sb("hot_ids16", [K, HOT * P], fp16)
        onehot = sb("onehot", [K, CH * HOT * P], bf16)
        feats = [sb(f"feats{u}", [P, P * PAD]) for u in range(2)]
        dots = [sb(f"dots{u}", [PAD, (NF - 1) * P]) for u in range(2)]
        z = [sb(f"z{u}", [P, ZC * P]) for u in range(2)]
        w1a = sb("w1a", [P, N1])
        w1b = sb("w1b", [P, N1])
        w1d = sb("w1d", [P, N1])
        w1z = sb("w1z", [P, ZC * N1])
        w2 = sb("w2", [P, C1 * N2])
        w3 = sb("w3", [P, C2])
        b1 = sb("b1", [P, C1])
        b2 = sb("b2", [P, C2])
        h1 = sb("h1", [P, C1 * P])
        h2 = sb("h2", [P, C2 * P])
        h2w = sb("h2w", [P, P])
        ones = sb("ones", [P, 1])
        y = sb("y", [P, TILES])

        tp = [ctx.enter_context(nc.psum_tensor(f"tp{b}", [P, 512], fp32)) for b in range(2)]
        gp = [ctx.enter_context(nc.psum_tensor(f"gp{b}", [P, HALF * P], fp32)) for b in range(2)]
        h1p = ctx.enter_context(nc.psum_tensor("h1p", [P, C1 * P], fp32))
        h2p = ctx.enter_context(nc.psum_tensor("h2p", [P, 512], fp32))
        yp = h2p[:, C2 * P:C2 * P + TILES]

        first_ids_loaded = sem("first_ids_loaded")
        ids_loaded = sem("ids_loaded")
        dense_loaded = sem("dense_loaded")
        table_loaded = [sem(f"table_loaded{s}") for s in range(HOT)]
        weights_loaded = sem("weights_loaded")
        row_of_ready = sem("row_of_ready")
        ident_ready = sem("ident_ready")
        setup_done = sem("setup_done")
        split = [sem(f"split{i}") for i in range(3)]
        split_rest = sem("split_rest")
        w1d_ready = sem("w1d_ready")
        w1z_zeroed = sem("w1z_zeroed")
        idx_staged = sem("idx_staged")
        dense_placed = sem("dense_placed")
        hot_ids_loaded = [sem(f"hot_ids_loaded{u}") for u in range(2)]
        hot_ids16_ready = sem("hot_ids16_ready")
        tiles_begun = sem("tiles_begun")
        gathered = [[sem(f"gathered{u}_{i}") for i in range(len(groups))] for u in range(2)]
        tp_ready = [sem(f"tp_ready{b}") for b in range(2)]
        tp_copied = [sem(f"tp_copied{b}") for b in range(2)]
        onehot_ready = sem("onehot_ready")
        gram_ready = sem("gram_ready")
        gram_copied_dve = sem("gram_copied_dve")
        gram_copied_act = sem("gram_copied_act")
        packed = [sem(f"packed{u}") for u in range(2)]
        last_packed = [sem(f"last_packed{c}") for c in range(ZC)]
        packed_by_pool = [sem(f"packed_by_pool{u}") for u in range(2)]
        h1_ready = sem("h1_ready")
        h1_relu = sem("h1_relu")
        h2_ready = sem("h2_ready")
        h2_relu = sem("h2_relu")
        h2_scaled = sem("h2_scaled")
        h2w_ready = sem("h2w_ready")
        last_h1_ready = sem("last_h1_ready")
        last_h2_ready = sem("last_h2_ready")
        y_ready = sem("y_ready")
        y_copied = sem("y_copied")
        stored = sem("stored")

        w1 = io["W_top1"]
        weight_loads = [
            (w1a[:, :], w1[0:D, :]),
            (w1b[:, :], w1[D + PAIRS:, :]),
            (w2[:, :].rearrange("p (c n) -> p c n", c=C1), io["W_top2"].rearrange("(c p) n -> p c n", p=P)),
            (w3[:, :], io["W_top3"].rearrange("(c p) o -> p (c o)", p=P)),
            (b1[:, :], io["b_top1"].rearrange("(c p) -> p c", p=P)),
            (b2[:, :], io["b_top2"].rearrange("(c p) -> p c", p=P)),
        ]

        for f0, width, g0, n, c, row in pieces:
            for f in range(f0, f0 + width):
                g = max(g0, f + 1)
                if g < g0 + n:
                    first = D + f * (NF - 1) - f * (f - 1) // 2 + g - f - 1
                    at = row + (g - g0) * width + f - f0
                    weight_loads.append((w1z[at:row + n * width:width, c * N1:(c + 1) * N1],
                                         w1[first:first + g0 + n - g, :]))

        block = ctx.enter_context(nc.Block())

        def over_tiles(eng, tile, first=None, between=None):
            (first or tile)(0, 0, 0)
            tile(1, 0, 1)
            if between:
                between()
            with eng.Fori(1, TILES // 2 - 1) as k:
                tile(0, k, 2 * k)
                tile(1, k, 2 * k + 1)
            tile(0, TILES // 2 - 1, TILES - 2)
            tile(1, TILES // 2 - 1, TILES - 1)

        def there(t):
            return not isinstance(t, int) or 0 <= t < TILES

        def table_of(tensor, s):
            return tensor[:, s * CH * D:(s + 1) * CH * D]

        def last_h1p(c):
            return gp[c // 2][:, c % 2 * 512:c % 2 * 512 + P]

        def last_h2p(c):
            return (h2p, h1p)[c][:, 0:P]

        def load_hot_ids(eng, u, t):
            eng.dma_start(hot_ids[u][:, :], io["hot_ids"][bass.ds(t, 1), :].partition_broadcast(K)) \
               .then_inc(hot_ids_loaded[u], 16)

        def pack_piece(eng, u, piece, done):
            f, width, g, n, c, row = piece
            eng.dma_start(z[u][row:row + n * width, c * P:(c + 1) * P], dots[u][g:g + n, f * P:(f + width) * P]) \
               .then_inc(done, 16)

        @block.sync
        def _(sp):
            ids_by_tile = io["ids"].rearrange("(p t) f -> p (t f)", p=P)
            sp.dma_start(ids[:, :2 * FIELDS], ids_by_tile[:, :2 * FIELDS]).then_inc(first_ids_loaded, 16)

            for u in range(2):
                load_hot_ids(sp, u, u)
            for s, f in enumerate(hot):
                sp.dma_start(table_of(table, s).rearrange("k (c d) -> k c d", c=CH),
                             io[f"tbl_{f - 1}"].rearrange("(c k) d -> k c d", k=K)).then_inc(table_loaded[s], 16)
                if s == 2:
                    sp.dma_start(ids[:, 2 * FIELDS:], ids_by_tile[:, 2 * FIELDS:]).then_inc(ids_loaded, 16)
                    sp.dma_start(dense[:, :], io["dense_by_tile"][:, :]).then_inc(dense_loaded, 16)
            sp.wait_ge(w1z_zeroed, 1)
            with nc.allow_non_contiguous_dma(reason="biases and W_top3: a few words per partition, once"):
                for dst, src in weight_loads:
                    sp.dma_start(dst, src).then_inc(weights_loaded, 16)

            def pack(u, k, t):
                sp.wait_ge(gram_copied_dve, HALVES * (t + 1) + 2)
                sp.wait_ge(gram_copied_act, HALVES * (t + 1) + 2)
                for piece in pieces[:-BY_POOL] if not there(t + 2) else pieces:
                    pack_piece(sp, u, piece, packed[u] if there(t + 1) else last_packed[piece[4]])

            over_tiles(sp, pack)
            sp.wait_ge(y_copied, 1)
            sp.dma_start(io["out"].rearrange("(p t) o -> p (t o)", p=P), y[:, :]).then_inc(stored, 16)
            sp.wait_ge(stored, 16)

        @block.gpsimd
        def _(pool):
            def gather(u, k, t):
                pool.wait_ge(idx_staged, t + 1).then_inc(tiles_begun, 1)
                for i, group in enumerate(groups):
                    for f in group:
                        pool.indirect_dma_start(
                            rows[u][:, f * D:(f + 1) * D], None, io[f"tbl_{f - 1}"][:, :],
                            bass.IndirectOffsetOnAxis(idx[u][:, f - 1:f], 0)).then_inc(gathered[u][i], 16)

            pool.iota(row_of[:, :], [[K, CH]], base=0, channel_multiplier=1).then_inc(row_of_ready, 1)
            pool.memset(ident[:, :], 0.0).then_inc(ident_ready, 1)
            pool.wait_ge(ident_ready, 1)
            pool.affine_select(out=ident[:, :], in_=ident[:, :], compare_op=ALU.not_equal, fill=1.0, base=0,
                               pattern=[[-1, P]], channel_multiplier=1).then_inc(ident_ready, 1)
            over_tiles(pool, gather)
            for u in range(2):
                pool.wait_ge(gram_copied_dve, HALVES * (TILES - 1 + u) + 2)
                pool.wait_ge(gram_copied_act, HALVES * (TILES - 1 + u) + 2)
                for piece in pieces[-BY_POOL:]:
                    pack_piece(pool, u, piece, packed_by_pool[u])

        def copy_gram(copy, u, h, js):
            dst = dots[u][:, :].rearrange("g (f c j) -> g c f j", f=NF - 1, j=PER)
            src = gp[h % 2][:, :].rearrange("p (c n) -> p c n", c=HALF)
            for j in js:
                last = copy(dst[0:NF, h * HALF:(h + 1) * HALF, :, j],
                            src[j * PAD:j * PAD + NF, :, j * (NF - 1):(j + 1) * (NF - 1)])
            return last

        def copy_features(copy, u, b, fs):
            src = tp[b][:, :].rearrange("d (f b) -> d f b", b=P)
            dst = feats[u][:, :].rearrange("d (b f) -> d f b", f=PAD)
            for at, f, n, step in progressions(fs):
                last = copy(dst[:, f:f + (n - 1) * step + 1:step, :], src[:, at:at + n, :])
            return last

        def copy_group(copy, eng, b, u, t, i):
            eng.wait_ge(tp_ready[b], turn(b, t, i) + 1)
            copy_features(copy, u, b, groups[i]).then_inc(tp_copied[b], 1)

        def copy_onehot_features(copy, eng, b, u, t):
            eng.wait_ge(tp_ready[b], onehot_turn(b, t) + 1)
            copy_features(copy, u, b, hot_of[b]).then_inc(tp_copied[b], 1)

        @block.vector
        def _(dve):
            copy = dve.tensor_copy

            def stage_rows(u, t):
                copy(idx[u][:, :], ids[:, bass.ds(t * FIELDS, FIELDS)]).then_inc(idx_staged, 1)

            def make_onehot(u, t, first, last):
                if first == 0:
                    dve.wait_ge(hot_ids16_ready, t + 1)
                for c in range(first, last):
                    made = dve.tensor_tensor(
                        onehot[:, c * HOT * P:(c + 1) * HOT * P].rearrange("k (s b) -> k s b", b=P),
                        hot_ids16[:, :].rearrange("k (s b) -> k s b", b=P),
                        row_of16[:, c * P:(c + 1) * P].rearrange("k (s b) -> k s b", s=1).to_broadcast([K, HOT, P]),
                        ALU.is_equal)
                if last == CH:
                    made.then_inc(onehot_ready, 1)

            dve.sem_inc(tp_copied[0], 1)
            dve.sem_inc(gram_copied_dve, 2)
            dve.memset(w1z[:, :], 0.0).then_inc(w1z_zeroed, 1)
            dve.wait_ge(first_ids_loaded, 16)
            for u in range(2):
                stage_rows(u, u)
            for u in range(2):
                dve.memset(feats[u][:, :].rearrange("d (b f) -> d b f", f=PAD)[:, :, NF:], 0.0).then_inc(setup_done, 1)
            dve.memset(ones[:, :], 1.0).then_inc(setup_done, 1)
            dve.wait_ge(row_of_ready, 1)
            for c in range(CH):
                last = copy(row_of16[:, c * P:(c + 1) * P], row_of[0:K, c:c + 1].to_broadcast([K, P]))
            last.then_inc(setup_done, 1)
            dve.wait_ge(setup_done, 4)
            make_onehot(0, 0, 0, CH)
            def relu2(t):
                dve.wait_ge(h2_ready, t + 1)
                for c in range(C2):
                    dve.tensor_scalar(h2[:, c * P:(c + 1) * P], h2p[:, c * P:(c + 1) * P], b2[:, c:c + 1], 0.0,
                                      ALU.add, ALU.max).then_inc(h2_relu, 1)
                dve.wait_ge(h2_relu, C2 * (t + 1))
                dve.tensor_tensor(h2w[:, :], h2[:, 0:P], w3[:, 0:1].to_broadcast([P, P]), ALU.mult) \
                   .then_inc(h2_scaled, 1)
                dve.wait_ge(h2_scaled, t + 1)
                dve.scalar_tensor_tensor(h2w[:, :], h2[:, P:2 * P], w3[:, 1:2], h2w[:, :], ALU.mult, ALU.add) \
                   .then_inc(h2w_ready, 1)

            def next_rows(u, t):
                if there(t + 2):
                    dve.wait_ge(tp_ready[1], turn(1, t, 5) + 1)
                    stage_rows(u, t + 2)

            def tile0(u, k, t):
                for s in range(HOT + 1):
                    if s < HOT:
                        dve.wait_ge(split[0], s + 1)
                        dve.tensor_tensor(table_of(table, s), table_of(table, s), table_of(parts[0], s),
                                          ALU.subtract).then_inc(split_rest, 1)
                    if s:
                        dve.wait_ge(split[1], s)
                        dve.tensor_tensor(table_of(parts[2], s - 1), table_of(table, s - 1),
                                          table_of(parts[1], s - 1), ALU.subtract).then_inc(split[2], 1)
                    if s == 1:
                        copy_group(copy, dve, 0, 0, 0, 0)
                    if s == 3:
                        copy_group(copy, dve, 0, 0, 0, 2)
                copy_group(copy, dve, 0, 0, 0, 4)
                dve.wait_ge(ids_loaded, 16)
                next_rows(0, 0)
                copy_onehot_features(copy, dve, 0, 0, 0)
                make_onehot(1, 1, 0, CH // 2)
                for h in range(HALVES):
                    dve.wait_ge(gram_ready, h + 1)
                    copy_gram(copy, 0, h, (0, 1)).then_inc(gram_copied_dve, 1)
                    if h == 2:
                        dve.wait_ge(weights_loaded, 16 * len(weight_loads))
                        dve.tensor_tensor(w1d[:, :], w1a[:, :], w1b[:, :], ALU.add).then_inc(w1d_ready, 1)
                    if h < 2:
                        make_onehot(1, 1, CH // 2 + h * CH // 4, CH // 2 + (h + 1) * CH // 4)
                copy_onehot_features(copy, dve, 0, 1, 1)
                make_onehot(0, 2, 0, CH // 4)

            def tile(u, k, t):
                for i in (0, 2, 4):
                    copy_group(copy, dve, 0, u, t, i)
                    if isinstance(t, int) and t == 1:
                        make_onehot(0, 2, (i // 2 + 1) * CH // 4, (i // 2 + 2) * CH // 4)
                next_rows(u, t)
                if there(t + 1):
                    copy_onehot_features(copy, dve, 0, 1 - u, t + 1)
                if there(t - 2) and there(t + 1):
                    relu2(t - 2)
                for h in range(HALVES):
                    dve.wait_ge(gram_ready, HALVES * t + h + 1)
                    copy_gram(copy, u, h, (0, 1)).then_inc(gram_copied_dve, 1)
                    if there(t + 2):
                        make_onehot(u, t + 2, h * CH // HALVES, (h + 1) * CH // HALVES)

            over_tiles(dve, tile, tile0)
            relu2(TILES - 3)
            relu2(TILES - 2)
            for c in range(1, C1, 2):
                dve.wait_ge(last_h1_ready, c + 1)
                dve.tensor_scalar(h1[:, c * P:(c + 1) * P], last_h1p(c), b1[:, c:c + 1], 0.0, ALU.add, ALU.max) \
                   .then_inc(h1_relu, 1)
            for c in range(C2):
                dve.wait_ge(last_h2_ready, c + 1)
                dve.tensor_scalar(h2[:, c * P:(c + 1) * P], last_h2p(c), b2[:, c:c + 1], 0.0, ALU.add, ALU.max) \
                   .then_inc(h2_relu, 1)
            dve.wait_ge(y_ready, TILES)
            copy(y[:, :], yp).then_inc(y_copied, 1)

        @block.scalar
        def _(act):
            act.sem_inc(tp_copied[1], 1)
            act.sem_inc(gram_copied_act, 2)
            act.wait_ge(setup_done, 4)

            def copy(dst, src):
                return act.activation(dst, src, ACT.Copy)

            def convert_ids(u, k, t):
                act.wait_ge(hot_ids_loaded[u], 16 * (k + 1))
                if not isinstance(t, int) or t > 0:
                    act.wait_ge(onehot_ready, t)
                copy(hot_ids16[:, :], hot_ids[u][:, :]).then_inc(hot_ids16_ready, 1)

            convert_ids(0, 0, 0)
            def relu1(t):
                act.wait_ge(h1_ready, t + 1)
                for c in range(C1):
                    act.activation(h1[:, c * P:(c + 1) * P], h1p[:, c * P:(c + 1) * P], ACT.Relu,
                                   bias=b1[:, c:c + 1]).then_inc(h1_relu, 1)

            def place_dense(u, t):
                copy(feats[u][:, 0:(P - 1) * PAD + 1:PAD], dense[:, bass.ds(t * P, P)]).then_inc(dense_placed, 1)

            def next_ids(u, t):
                if there(t + 2):
                    act.wait_ge(hot_ids16_ready, t + 1)
                    load_hot_ids(act, u, t + 2)

            def copy_grams(u, t):
                for h in range(HALVES):
                    act.wait_ge(gram_ready, HALVES * t + h + 1)
                    copy_gram(copy, u, h, (2, 3)).then_inc(gram_copied_act, 1)

            def tile0(u, k, t):
                next_ids(0, 0)
                for s in range(HOT + 1):
                    if s < HOT:
                        act.wait_ge(table_loaded[s], 16)
                        copy(table_of(parts[0], s), table_of(table, s)).then_inc(split[0], 1)
                    if s:
                        act.wait_ge(split_rest, s)
                        copy(table_of(parts[1], s - 1), table_of(table, s - 1)).then_inc(split[1], 1)
                    if s == 2:
                        copy_group(copy, act, 1, 0, 0, 1)
                copy_group(copy, act, 1, 0, 0, 3)
                copy_group(copy, act, 1, 0, 0, 5)
                copy_onehot_features(copy, act, 1, 0, 0)
                act.wait_ge(dense_loaded, 16)
                place_dense(0, 0)
                convert_ids(1, 0, 1)
                copy_grams(0, 0)
                copy_onehot_features(copy, act, 1, 1, 1)
                convert_ids(0, 1, 2)

            def tile(u, k, t):
                next_ids(u, t)
                place_dense(u, t)
                for what in TURNS[1]:
                    if what == "onehot":
                        if there(t + 1):
                            copy_onehot_features(copy, act, 1, 1 - u, t + 1)
                    else:
                        copy_group(copy, act, 1, u, t, what)
                    if what == 5 and there(t - 2):
                        relu1(t - 2)
                if there(t + 2):
                    convert_ids(u, k + 1, t + 2)
                copy_grams(u, t)

            def weights_here():
                act.wait_ge(weights_loaded, 16 * len(weight_loads))

            over_tiles(act, tile, tile0, weights_here)
            relu1(TILES - 2)
            for c in range(0, C1, 2):
                act.wait_ge(last_h1_ready, c + 1)
                act.activation(h1[:, c * P:(c + 1) * P], last_h1p(c), ACT.Relu, bias=b1[:, c:c + 1]) \
                   .then_inc(h1_relu, 1)

        @block.tensor
        def _(pe):
            def onehot_products(b, u, t):
                pe.wait_ge(onehot_ready, t + 1)
                pe.wait_ge(tp_copied[b], onehot_turn(b, t) + 1)
                for s in range(len(hot_of[b])):
                    for c in range(CH):
                        for i, part in enumerate(parts):
                            at = ((b * HA + s) * CH + c) * D
                            hots = (c * HOT + b * HA + s) * P
                            last = pe.matmul(tp[b][:, s * P:(s + 1) * P], part[:, at:at + D],
                                             onehot[:, hots:hots + P], start=c == 0 and i == 0,
                                             stop=c == CH - 1 and i == 2)
                last.then_inc(tp_ready[b], 1)

            def transposes(u, k, t, i):
                b = i % 2
                pe.wait_ge(gathered[u][i], 16 * len(groups[i]) * (k + 1))
                pe.wait_ge(tp_copied[b], turn(b, t, i) + 1)
                for m, f in enumerate(groups[i]):
                    last = pe.transpose(tp[b][:, m * P:(m + 1) * P], rows[u][:, f * D:(f + 1) * D], ident[:, :])
                last.then_inc(tp_ready[b], 1)

            def gram_wait(t):
                pe.wait_ge(dense_placed, t + 1)
                pe.wait_ge(tp_copied[0], turn(0, t, 4) + 2)
                pe.wait_ge(tp_copied[1], turn(1, t, 5) + 2)

            def gram_half(u, t, h):
                pe.wait_ge(gram_copied_dve, HALVES * t + h + 1)
                pe.wait_ge(gram_copied_act, HALVES * t + h + 1)
                batch = feats[u][:, :].rearrange("d (b f) -> d b f", f=PAD)
                for c in range(HALF):
                    b = (h * HALF + c) * PER
                    last = pe.matmul(gp[h % 2][0:P - PAD + NF, c * P:c * P + PER * (NF - 1)],
                                     feats[u][:, b * PAD:(b + PER - 1) * PAD + NF], batch[:, b:b + PER, 0:NF - 1],
                                     start=True, stop=True)
                last.then_inc(gram_ready, 1)

            def layer1_wait(u, k):
                shared = isinstance(k, int) and k == TILES // 2 - 1
                pe.wait_ge(packed[u], 16 * (len(pieces) * (k + 1) - (BY_POOL if shared else 0)))
                if shared:
                    pe.wait_ge(packed_by_pool[u], 16 * BY_POOL)

            def layer1_chunk(u, t, c, out):
                pe.matmul(out, w1d[:, c * P:(c + 1) * P], dense[:, bass.ds(t * P, P)], start=True, stop=False)
                for q in range(ZC):
                    last = pe.matmul(out, w1z[0:zrows[q], q * N1 + c * P:q * N1 + (c + 1) * P],
                                     z[u][0:zrows[q], q * P:(q + 1) * P], start=False, stop=q == ZC - 1)
                return last

            def layer2_wait(t):
                pe.wait_ge(h1_relu, C1 * (t + 1))

            def layer2_chunk(c, out):
                for q in range(C1):
                    last = pe.matmul(out, w2[:, q * N2 + c * P:q * N2 + (c + 1) * P],
                                     h1[:, q * P:(q + 1) * P], start=q == 0, stop=q == C1 - 1)
                return last

            def layer2(t):
                layer2_wait(t)
                for c in range(C2):
                    last = layer2_chunk(c, h2p[:, c * P:(c + 1) * P])
                last.then_inc(h2_ready, 1)

            def layer3(t):
                pe.wait_ge(h2w_ready, t + 1)
                pe.matmul(yp[:, bass.ds(t, 1)], h2w[:, :], ones[:, :], start=True, stop=True).then_inc(y_ready, 1)

            def last_layer3(t):
                pe.wait_ge(h2_relu, C2 * (t + 1))
                for c in range(C2):
                    last = pe.matmul(yp[:, bass.ds(t, 1)], h2[:, c * P:(c + 1) * P], w3[:, c:c + 1],
                                     start=c == 0, stop=c == C2 - 1)
                last.then_inc(y_ready, 1)

            pe.wait_ge(ident_ready, 2)
            pe.wait_ge(setup_done, 4)

            def tile0(u, k, t):
                for i in range(len(groups)):
                    transposes(0, 0, 0, i)
                pe.wait_ge(split[2], HOT)
                for b in (1, 0):
                    onehot_products(b, 0, 0)
                pe.wait_ge(tp_copied[0], onehot_turn(0, 0) + 2)
                pe.wait_ge(tp_copied[1], onehot_turn(1, 0) + 2)
                pe.wait_ge(dense_placed, 1)
                for h in range(HALVES):
                    gram_half(0, 0, h)
                for b in (1, 0):
                    onehot_products(b, 1, 1)

            def tile(u, k, t):
                behind = there(t - 2)
                if behind:
                    layer1_wait(u, k - 1)
                for i in range(len(groups)):
                    transposes(u, k, t, i)
                    if behind and i in LAYER1_AFTER:
                        c = LAYER1_AFTER.index(i)
                        last = layer1_chunk(u, t - 2, c, h1p[:, c * P:(c + 1) * P])
                if behind:
                    last.then_inc(h1_ready, 1)
                if there(t + 1):
                    onehot_products(1, 1 - u, t + 1)
                    onehot_products(0, 1 - u, t + 1)
                if behind and there(t + 1):
                    layer2(t - 2)
                gram_wait(t)
                gram_half(u, t, 0)
                if behind and there(t + 1):
                    layer3(t - 2)
                for h in range(1, HALVES):
                    gram_half(u, t, h)

            def weights_here():
                pe.wait_ge(w1d_ready, 1)
                pe.wait_ge(weights_loaded, 16 * len(weight_loads))

            over_tiles(pe, tile, tile0, weights_here)
            layer2(TILES - 3)
            layer1_wait(0, TILES // 2 - 1)
            for c in range(C1):
                last = layer1_chunk(0, TILES - 2, c, h1p[:, c * P:(c + 1) * P])
            last.then_inc(h1_ready, 1)
            layer3(TILES - 3)
            pe.wait_ge(gram_copied_dve, HALVES * TILES + 2)
            pe.wait_ge(gram_copied_act, HALVES * TILES + 2)
            for c in range(C1):
                pe.matmul(last_h1p(c), w1d[:, c * P:(c + 1) * P], dense[:, (TILES - 1) * P:], start=True, stop=False)
            for q, n in enumerate(zrows):
                if q == 1:
                    layer2(TILES - 2)
                if q == ZC - 1:
                    pe.wait_ge(packed_by_pool[1], 16 * BY_POOL)
                pe.wait_ge(last_packed[q], 16 * sum(piece[4] == q for piece in pieces[:-BY_POOL]))
                for c in range(C1):
                    last = pe.matmul(last_h1p(c), w1z[0:n, q * N1 + c * P:q * N1 + (c + 1) * P],
                                     z[1][0:n, q * P:(q + 1) * P], start=False, stop=q == ZC - 1)
                    if q == ZC - 1:
                        last.then_inc(last_h1_ready, 1)
            layer3(TILES - 2)
            layer2_wait(TILES - 1)
            for c in range(C2):
                layer2_chunk(c, last_h2p(c)).then_inc(last_h2_ready, 1)
            last_layer3(TILES - 1)


def kernel(**inputs):
    import concourse.bacc as bacc
    from concourse.bass_utils import run_bass_kernel_spmd

    nc = bacc.Bacc("TRN2", target_bir_lowering=False, num_devices=1)
    arrays, io = {}, {}
    for name, a in inputs.items():
        if name == "r_dense_features":
            continue
        a = np.ascontiguousarray(a)
        arrays["in_" + name] = a
        io[name] = nc.dram_tensor("in_" + name, a.shape, mybir.dt.from_np(a.dtype), kind="ExternalInput").ap()
    batch, d = inputs["r_dense_features"].shape
    dense = np.ascontiguousarray(
        np.asarray(inputs["r_dense_features"]).reshape(P, batch // P, d).transpose(2, 1, 0).reshape(d, batch))
    arrays["in_dense_by_tile"] = dense
    io["dense_by_tile"] = nc.dram_tensor("in_dense_by_tile", dense.shape, mybir.dt.from_np(dense.dtype),
                                         kind="ExternalInput").ap()
    hot = hot_features([inputs[f"tbl_{i}"].shape[0] for i in range(inputs["ids"].shape[1])])
    hot_ids = np.asarray(inputs["ids"])[:, [f - 1 for f in hot]].reshape(P, batch // P, len(hot)).transpose(1, 2, 0)
    hot_ids = np.ascontiguousarray(hot_ids.reshape(batch // P, len(hot) * P))
    arrays["in_hot_ids"] = hot_ids
    io["hot_ids"] = nc.dram_tensor("in_hot_ids", hot_ids.shape, mybir.dt.from_np(hot_ids.dtype),
                                   kind="ExternalInput").ap()
    io["out"] = nc.dram_tensor("out_0", (batch, 1), mybir.dt.float32, kind="ExternalOutput").ap()
    build(nc, io)
    r = run_bass_kernel_spmd(nc, [arrays], core_ids=[0])
    return r.results[0]["out_0"]
```
